# Optimizing a Trainium2 kernel written in Bass

```python
import numpy as np
import jax
import jax.numpy as jnp

def _softmax(x, axis=-1):
    return jax.nn.softmax(x, axis=axis)

def _gelu(x):
    return jax.nn.gelu(x, approximate=True)

def _silu(x):
    return jax.nn.silu(x)

def _sigmoid(x):
    return jax.nn.sigmoid(x)

def _layernorm(x, axis=-1, eps=1e-05):
    m = jnp.mean(x, axis=axis, keepdims=True)
    v = jnp.var(x, axis=axis, keepdims=True)
    return (x - m) / jnp.sqrt(v + eps)

def _scatter_add(tgt, idx, src, axis=0):
    return tgt.at[idx].add(src)

def _segment_sum(src, seg, n):
    return jax.ops.segment_sum(src, seg, n)
kernel_name = 'mk_recurrent_d1_jaxref_r8_9fa15f'

def setup_inputs(seed: int=0):
    np.random.seed(seed)
    _w = jnp.asarray

    def _L0_attn_setup():
        import jax, jax.numpy as jnp
        import numpy as np
        DM, EXP, N, K, FRAC = (128, 2, 16, 4, 16)
        D = DM * EXP
        DTR = D // FRAC
        EPS = 1e-06

        def _mamba_block(x, rms_w, in_W, in_b, conv_w, conv_b, A_log, dbc_W, dbc_b, dup_W, dup_b, out_W, out_b):
            residual = x
            h = x * jax.lax.rsqrt(jnp.mean(x * x, axis=-1, keepdims=True) + EPS) * rms_w
            proj = h @ in_W + in_b
            x1, g = (proj[..., :D], proj[..., D:])
            xt = jnp.transpose(x1, (0, 2, 1))
            xc = jax.lax.conv_general_dilated(xt, conv_w[:, None, :], window_strides=(1,), padding=[(K - 1, 0)], feature_group_count=D, dimension_numbers=('NCH', 'OIH', 'NCH'))
            xc = xc + conv_b[:, None]
            x1 = jax.nn.silu(jnp.transpose(xc, (0, 2, 1)))
            A = -jnp.exp(A_log)
            dbc = x1 @ dbc_W + dbc_b
            delta, Bm, Cm = (dbc[..., :DTR], dbc[..., DTR:DTR + N], dbc[..., DTR + N:])
            delta = jax.nn.softplus(delta @ dup_W + dup_b)
            A_disc = jnp.exp(delta[..., None] * A)
            B_x = delta[..., None] * Bm[:, :, None, :] * x1[..., None]
            Ad_t = jnp.transpose(A_disc, (1, 0, 2, 3))
            Bx_t = jnp.transpose(B_x, (1, 0, 2, 3))

            def step(hc, inp):
                a, b = inp
                hc = a * hc + b
                return (hc, hc)
            h0 = jnp.zeros((x.shape[0], D, N), x1.dtype)
            _, hs = jax.lax.scan(step, h0, (Ad_t, Bx_t))
            y = jnp.einsum('tbdn,btn->btd', hs, Cm)
            y = jax.nn.silu(g) * y
            out = y @ out_W + out_b
            return out + residual
        key = jax.random.key(seed)
        ks = jax.random.split(key, 12)
        s = lambda fan: 1.0 / np.sqrt(fan)
        x = jax.random.normal(ks[0], (2, 128, DM), jnp.float32)
        rms_w = jnp.ones((DM,), jnp.float32)
        in_W = jax.random.normal(ks[1], (DM, 2 * D), jnp.float32) * s(DM)
        in_b = jax.random.normal(ks[2], (2 * D,), jnp.float32) * s(DM)
        conv_w = jax.random.normal(ks[3], (D, K), jnp.float32) * s(K)
        conv_b = jax.random.normal(ks[4], (D,), jnp.float32) * s(K)
        A_log = jnp.log(jnp.tile(jnp.arange(1, N + 1, dtype=jnp.float32), (D, 1)))
        dbc_W = jax.random.normal(ks[5], (D, DTR + 2 * N), jnp.float32) * s(D)
        dbc_b = jax.random.normal(ks[6], (DTR + 2 * N,), jnp.float32) * s(D)
        dup_W = jax.random.normal(ks[7], (DTR, D), jnp.float32) * s(DTR)
        dup_b = jax.random.normal(ks[8], (D,), jnp.float32) * s(DTR)
        out_W = jax.random.normal(ks[9], (D, DM), jnp.float32) * s(D)
        out_b = jax.random.normal(ks[10], (DM,), jnp.float32) * s(D)
        return dict(x=x, rms_w=rms_w, in_W=in_W, in_b=in_b, conv_w=conv_w, conv_b=conv_b, A_log=A_log, dbc_W=dbc_W, dbc_b=dbc_b, dup_W=dup_W, dup_b=dup_b, out_W=out_W, out_b=out_b)
    _L0_attn_in = _L0_attn_setup()

    def _L0_ffn_setup():
        import jax, jax.numpy as jnp
        import numpy as np
        DIM = 128
        DEPTH = 6
        HEADS = 16
        DIM_HEAD = 64
        WINDOW = 32
        INNER = HEADS * DIM_HEAD
        DIM_INNER = int(DIM * 4 * 2 / 3)
        QK_SCALE = 8.0

        def shift_tokens(t):
            a, s = jnp.split(t, 2, -1)
            s = jnp.pad(s, ((0, 0), (1, 0), (0, 0)))[:, :-1]
            return jnp.concatenate([a, s], -1)

        def l2norm(t):
            return t / jnp.maximum(jnp.linalg.norm(t, axis=-1, keepdims=True), 1e-12)

        def rotate_half(x):
            x1, x2 = jnp.split(x, 2, -1)
            return jnp.concatenate([-x2, x1], -1)

        def rotary_tables(n):
            half = jnp.arange(0, DIM_HEAD, 2, dtype=jnp.float32)
            inv_freq = 1.0 / 10000.0 ** (half / DIM_HEAD)
            t = jnp.arange(n, dtype=jnp.float32)
            freqs = t[:, None] * inv_freq[None, :]
            freqs = jnp.concatenate([freqs, freqs], -1)
            base_scale = (half + 0.4 * DIM_HEAD) / (1.4 * DIM_HEAD)
            power = (t - n // 2) / (WINDOW // 2)
            scale = base_scale[None, :] ** power[:, None]
            scale = jnp.concatenate([scale, scale], -1)
            return (freqs, scale)

        def local_attention(q, k, v):
            b, h, n, d = q.shape
            w = WINDOW
            nw = n // w
            bq = q.reshape(b, h, nw, w, d)
            bk = k.reshape(b, h, nw, w, d)
            bv = v.reshape(b, h, nw, w, d)

            def look(t):
                p = jnp.pad(t, ((0, 0), (0, 0), (1, 0), (0, 0), (0, 0)))
                return jnp.concatenate([p[:, :, :nw], p[:, :, 1:]], axis=3)
            bk2, bv2 = (look(bk), look(bv))
            seq = jnp.arange(n).reshape(nw, w)
            seq_p = jnp.pad(seq, ((1, 0), (0, 0)), constant_values=-1)
            jt = jnp.concatenate([seq_p[:nw], seq_p[1:]], axis=1)
            it = seq[:, :, None]
            jb = jt[:, None, :]
            mask = (it < jb) | (it > jb + w) | (jb == -1)
            sim = jnp.einsum('bhwie,bhwje->bhwij', bq, bk2) * QK_SCALE
            sim = jnp.where(mask, -jnp.finfo(sim.dtype).max, sim)
            attn = jax.nn.softmax(sim, -1)
            out = jnp.einsum('bhwij,bhwje->bhwie', attn, bv2)
            return out.reshape(b, h, n, d)

        def attn_layer(x, Wqkv, qs, ksc, Wo):
            b, n, _ = x.shape
            qkv = x @ Wqkv
            q, k, v = jnp.split(qkv, 3, -1)
            sh = lambda t: t.reshape(b, n, HEADS, DIM_HEAD).transpose(0, 2, 1, 3)
            q, k, v = (sh(q), sh(k), sh(v))
            q = l2norm(q) * qs
            k = l2norm(k) * ksc
            freqs, scale = rotary_tables(n)
            cos, sin = (jnp.cos(freqs), jnp.sin(freqs))
            q = q * cos * scale + rotate_half(q) * sin * scale
            inv = 1.0 / scale
            k = k * cos * inv + rotate_half(k) * sin * inv
            out = local_attention(q, k, v)
            out = out.transpose(0, 2, 1, 3).reshape(b, n, INNER)
            return out @ Wo

        def ffn_layer(x, g, bln, W1, b1, W2, b2):
            mu = x.mean(-1, keepdims=True)
            var = ((x - mu) ** 2).mean(-1, keepdims=True)
            xn = (x - mu) / jnp.sqrt(var + 1e-05) * g + bln
            hg = xn @ W1 + b1
            a, gate = jnp.split(hg, 2, -1)
            return a * jax.nn.gelu(gate, approximate=False) @ W2 + b2
        key = jax.random.key(seed)
        ks = jax.random.split(key, 8)
        B, N = (2, 256)
        init = lambda k, shape: jax.random.normal(k, shape, jnp.float32) * 0.02
        return {'x': jax.random.normal(ks[0], (B, N, DIM), jnp.float32), 'Wqkv': init(ks[1], (DEPTH, DIM, 3 * INNER)), 'q_scale': jnp.ones((DEPTH, DIM_HEAD), jnp.float32), 'k_scale': jnp.ones((DEPTH, DIM_HEAD), jnp.float32), 'Wo': init(ks[2], (DEPTH, INNER, DIM)), 'ln_g': jnp.ones((DEPTH, DIM), jnp.float32), 'ln_b': jnp.zeros((DEPTH, DIM), jnp.float32), 'W1': init(ks[3], (DEPTH, DIM, 2 * DIM_INNER)), 'b1': jnp.zeros((DEPTH, 2 * DIM_INNER), jnp.float32), 'W2': init(ks[4], (DEPTH, DIM_INNER, DIM)), 'b2': jnp.zeros((DEPTH, DIM), jnp.float32)}
    _L0_ffn_in = _L0_ffn_setup()
    _d = {'L0_attn_x': _L0_attn_in['x'], 'L0_attn_rms_w': _L0_attn_in['rms_w'], 'L0_attn_in_W': _L0_attn_in['in_W'], 'L0_attn_in_b': _L0_attn_in['in_b'], 'L0_attn_conv_w': _L0_attn_in['conv_w'], 'L0_attn_conv_b': _L0_attn_in['conv_b'], 'L0_attn_A_log': _L0_attn_in['A_log'], 'L0_attn_dbc_W': _L0_attn_in['dbc_W'], 'L0_attn_dbc_b': _L0_attn_in['dbc_b'], 'L0_attn_dup_W': _L0_attn_in['dup_W'], 'L0_attn_dup_b': _L0_attn_in['dup_b'], 'L0_attn_out_W': _L0_attn_in['out_W'], 'L0_attn_out_b': _L0_attn_in['out_b'], 'L0_ffn_Wqkv': _L0_ffn_in['Wqkv'], 'L0_ffn_q_scale': _L0_ffn_in['q_scale'], 'L0_ffn_k_scale': _L0_ffn_in['k_scale'], 'L0_ffn_Wo': _L0_ffn_in['Wo'], 'L0_ffn_ln_g': _L0_ffn_in['ln_g'], 'L0_ffn_ln_b': _L0_ffn_in['ln_b'], 'L0_ffn_W1': _L0_ffn_in['W1'], 'L0_ffn_b1': _L0_ffn_in['b1'], 'L0_ffn_W2': _L0_ffn_in['W2'], 'L0_ffn_b2': _L0_ffn_in['b2']}
    _x0 = _d['L0_attn_x']
    _d['L0_attn_x'] = jax.random.normal(jax.random.fold_in(jax.random.key(seed), 1), (8, 256, 128), dtype=_x0.dtype)
    del _x0
    return _d

def reference(L0_attn_x, L0_attn_rms_w, L0_attn_in_W, L0_attn_in_b, L0_attn_conv_w, L0_attn_conv_b, L0_attn_A_log, L0_attn_dbc_W, L0_attn_dbc_b, L0_attn_dup_W, L0_attn_dup_b, L0_attn_out_W, L0_attn_out_b, L0_ffn_Wqkv, L0_ffn_q_scale, L0_ffn_k_scale, L0_ffn_Wo, L0_ffn_ln_g, L0_ffn_ln_b, L0_ffn_W1, L0_ffn_b1, L0_ffn_W2, L0_ffn_b2):

    def _L0_attn_ref(x, rms_w, in_W, in_b, conv_w, conv_b, A_log, dbc_W, dbc_b, dup_W, dup_b, out_W, out_b):
        import jax, jax.numpy as jnp
        import numpy as np
        DM, EXP, N, K, FRAC = (128, 2, 16, 4, 16)
        D = DM * EXP
        DTR = D // FRAC
        EPS = 1e-06

        def _mamba_block(x, rms_w, in_W, in_b, conv_w, conv_b, A_log, dbc_W, dbc_b, dup_W, dup_b, out_W, out_b):
            residual = x
            h = x * jax.lax.rsqrt(jnp.mean(x * x, axis=-1, keepdims=True) + EPS) * rms_w
            proj = h @ in_W + in_b
            x1, g = (proj[..., :D], proj[..., D:])
            xt = jnp.transpose(x1, (0, 2, 1))
            xc = jax.lax.conv_general_dilated(xt, conv_w[:, None, :], window_strides=(1,), padding=[(K - 1, 0)], feature_group_count=D, dimension_numbers=('NCH', 'OIH', 'NCH'))
            xc = xc + conv_b[:, None]
            x1 = jax.nn.silu(jnp.transpose(xc, (0, 2, 1)))
            A = -jnp.exp(A_log)
            dbc = x1 @ dbc_W + dbc_b
            delta, Bm, Cm = (dbc[..., :DTR], dbc[..., DTR:DTR + N], dbc[..., DTR + N:])
            delta = jax.nn.softplus(delta @ dup_W + dup_b)
            A_disc = jnp.exp(delta[..., None] * A)
            B_x = delta[..., None] * Bm[:, :, None, :] * x1[..., None]
            Ad_t = jnp.transpose(A_disc, (1, 0, 2, 3))
            Bx_t = jnp.transpose(B_x, (1, 0, 2, 3))

            def step(hc, inp):
                a, b = inp
                hc = a * hc + b
                return (hc, hc)
            h0 = jnp.zeros((x.shape[0], D, N), x1.dtype)
            _, hs = jax.lax.scan(step, h0, (Ad_t, Bx_t))
            y = jnp.einsum('tbdn,btn->btd', hs, Cm)
            y = jax.nn.silu(g) * y
            out = y @ out_W + out_b
            return out + residual
        return _mamba_block(x, rms_w, in_W, in_b, conv_w, conv_b, A_log, dbc_W, dbc_b, dup_W, dup_b, out_W, out_b)

    def _L0_ffn_ref(x, Wqkv, q_scale, k_scale, Wo, ln_g, ln_b, W1, b1, W2, b2):
        import jax, jax.numpy as jnp
        import numpy as np
        DIM = 128
        DEPTH = 6
        HEADS = 16
        DIM_HEAD = 64
        WINDOW = 32
        INNER = HEADS * DIM_HEAD
        DIM_INNER = int(DIM * 4 * 2 / 3)
        QK_SCALE = 8.0

        def shift_tokens(t):
            a, s = jnp.split(t, 2, -1)
            s = jnp.pad(s, ((0, 0), (1, 0), (0, 0)))[:, :-1]
            return jnp.concatenate([a, s], -1)

        def l2norm(t):
            return t / jnp.maximum(jnp.linalg.norm(t, axis=-1, keepdims=True), 1e-12)

        def rotate_half(x):
            x1, x2 = jnp.split(x, 2, -1)
            return jnp.concatenate([-x2, x1], -1)

        def rotary_tables(n):
            half = jnp.arange(0, DIM_HEAD, 2, dtype=jnp.float32)
            inv_freq = 1.0 / 10000.0 ** (half / DIM_HEAD)
            t = jnp.arange(n, dtype=jnp.float32)
            freqs = t[:, None] * inv_freq[None, :]
            freqs = jnp.concatenate([freqs, freqs], -1)
            base_scale = (half + 0.4 * DIM_HEAD) / (1.4 * DIM_HEAD)
            power = (t - n // 2) / (WINDOW // 2)
            scale = base_scale[None, :] ** power[:, None]
            scale = jnp.concatenate([scale, scale], -1)
            return (freqs, scale)

        def local_attention(q, k, v):
            b, h, n, d = q.shape
            w = WINDOW
            nw = n // w
            bq = q.reshape(b, h, nw, w, d)
            bk = k.reshape(b, h, nw, w, d)
            bv = v.reshape(b, h, nw, w, d)

            def look(t):
                p = jnp.pad(t, ((0, 0), (0, 0), (1, 0), (0, 0), (0, 0)))
                return jnp.concatenate([p[:, :, :nw], p[:, :, 1:]], axis=3)
            bk2, bv2 = (look(bk), look(bv))
            seq = jnp.arange(n).reshape(nw, w)
            seq_p = jnp.pad(seq, ((1, 0), (0, 0)), constant_values=-1)
            jt = jnp.concatenate([seq_p[:nw], seq_p[1:]], axis=1)
            it = seq[:, :, None]
            jb = jt[:, None, :]
            mask = (it < jb) | (it > jb + w) | (jb == -1)
            sim = jnp.einsum('bhwie,bhwje->bhwij', bq, bk2) * QK_SCALE
            sim = jnp.where(mask, -jnp.finfo(sim.dtype).max, sim)
            attn = jax.nn.softmax(sim, -1)
            out = jnp.einsum('bhwij,bhwje->bhwie', attn, bv2)
            return out.reshape(b, h, n, d)

        def attn_layer(x, Wqkv, qs, ksc, Wo):
            b, n, _ = x.shape
            qkv = x @ Wqkv
            q, k, v = jnp.split(qkv, 3, -1)
            sh = lambda t: t.reshape(b, n, HEADS, DIM_HEAD).transpose(0, 2, 1, 3)
            q, k, v = (sh(q), sh(k), sh(v))
            q = l2norm(q) * qs
            k = l2norm(k) * ksc
            freqs, scale = rotary_tables(n)
            cos, sin = (jnp.cos(freqs), jnp.sin(freqs))
            q = q * cos * scale + rotate_half(q) * sin * scale
            inv = 1.0 / scale
            k = k * cos * inv + rotate_half(k) * sin * inv
            out = local_attention(q, k, v)
            out = out.transpose(0, 2, 1, 3).reshape(b, n, INNER)
            return out @ Wo

        def ffn_layer(x, g, bln, W1, b1, W2, b2):
            mu = x.mean(-1, keepdims=True)
            var = ((x - mu) ** 2).mean(-1, keepdims=True)
            xn = (x - mu) / jnp.sqrt(var + 1e-05) * g + bln
            hg = xn @ W1 + b1
            a, gate = jnp.split(hg, 2, -1)
            return a * jax.nn.gelu(gate, approximate=False) @ W2 + b2
        for i in range(DEPTH):
            x = attn_layer(shift_tokens(x), Wqkv[i], q_scale[i], k_scale[i], Wo[i]) + x
            x = ffn_layer(shift_tokens(x), ln_g[i], ln_b[i], W1[i], b1[i], W2[i], b2[i]) + x
        return x
    x = L0_attn_x
    xn = _layernorm(x, axis=-1)
    s = _L0_attn_ref(xn, L0_attn_rms_w, L0_attn_in_W, L0_attn_in_b, L0_attn_conv_w, L0_attn_conv_b, L0_attn_A_log, L0_attn_dbc_W, L0_attn_dbc_b, L0_attn_dup_W, L0_attn_dup_b, L0_attn_out_W, L0_attn_out_b)
    g = _silu(_L0_ffn_ref(xn, L0_ffn_Wqkv, L0_ffn_q_scale, L0_ffn_k_scale, L0_ffn_Wo, L0_ffn_ln_g, L0_ffn_ln_b, L0_ffn_W1, L0_ffn_b1, L0_ffn_W2, L0_ffn_b2))
    x = x + s * g
    return x

_drawn_inputs = setup_inputs


def setup_inputs(seed=0):
    import zlib

    import numpy as np

    out = dict(_drawn_inputs(seed))
    spreads = {'L0_attn_rms_w': (1.0, 0.2),
     'L0_ffn_q_scale': (1.0, 0.6),
     'L0_ffn_k_scale': (1.0, 0.6),
     'L0_ffn_ln_g': (1.0, 0.6),
     'L0_ffn_ln_b': (0.0, 0.8),
     'L0_ffn_b1': (0.0, 0.8),
     'L0_ffn_b2': (0.0, 0.1)}
    factors = {'L0_ffn_W1': 4.065, 'L0_ffn_W2': 4.029}
    for name, (base, spread) in spreads.items():
        noise = np.random.default_rng([zlib.crc32(name.encode()), seed]).standard_normal(out[name].shape)
        drawn = base * np.exp(spread * noise) if base else spread * noise
        out[name] = jnp.asarray(drawn.astype(out[name].dtype))
    for name, factor in factors.items():
        out[name] = (out[name] * factor).astype(out[name].dtype)
    return out
```

```python
from contextlib import ExitStack

import numpy as np

import concourse.bass as bass
from concourse import mybir

ALU = mybir.AluOpType
ACT = mybir.ActivationFunctionType
AX_X = mybir.AxisListType.X
F32 = mybir.dt.float32
BF16 = mybir.dt.bfloat16
F32R = mybir.dt.float32r

P = 128
LN_EXP = "natural_log_exp_and_others"
NB, SEQ, DM = 8, 256, 128
TILES = SEQ // P
DEPTH, HEADS, DH, WIN = 6, 16, 64, 32
INNER = HEADS * DH
GROUPS, GH = 4, 4
FFI = int(DM * 4 * 2 / 3)
FFC = [(0, 128), (128, 128), (256, FFI - 256)]
STEPS = DEPTH * NB
DI, NST, KC, DTR = 256, 16, 4, 16
DBLK = DI // P
NP_ = 4
PIECES = NST // NP_
QK_SCALE = 8.0
MASKED = -1e37
VH = DH + 1
MVEC = 10 + DBLK * (KC + NST)
NVEC = 9

QK = [f"QK{g}{t}" for g in range(4) for t in range(2)]
VS = [f"V{n}" for n in range(4)]
RING = {
    "pro": QK + VS,
    "first": ["QK00", "QK01", "QK10", "QK11", "QK20", "QK21", "OT0", "OT1", "QK30", "QK31", "OT2"] + VS,
    "mid": ["OT3p", "QK00", "QK01", "WOp", "QK10", "QK11", "VARp", "QK20", "QK21", "W1ap", "W1bp", "W1cp", "OT0",
            "W2p", "OT1", "QK30", "QK31", "OT2"] + VS,
    "last": ["OT3p", "WOp", "VARp", "W1ap", "W1bp", "W1cp", "OT0", "W2p", "OT1", "OT2"],
    "tail": ["OT3p", "WOp", "VARp", "W1ap", "W1bp", "W1cp", "W2p"],
}
GT = [f"{g}{t}" for g in range(4) for t in range(2)]
TRS = ["00", "01", "10", "11", "MEANp", "20", "21", "30", "31"]
DVE_LINKS = {"pro": 3, "first": 15, "mid": 20, "last": 17, "tail": 5}
KINDS = ["pro", "first", "mid", "last", "tail"]


def _sub(lists, keep):
    return {k: [e for e in v if keep(e)] for k, v in lists.items()}


def _per(pro, first, mid, last, tail):
    return dict(zip(KINDS, (pro, first, mid, last, tail)))


TRALL = _per([], [x for x in TRS if x != "MEANp"], TRS, TRS, ["MEANp"])
ATT = _per([], GT, GT, GT, [])
GRP = _per([], list("0123"), list("0123"), list("0123"), [])
NXT = _per(QK, QK, QK, [], [])
EV = {
    "ring_full": RING,
    "ring_act": _sub(RING, lambda e: e[:2] in ("OT", "QK", "W1") or e in VS),
    "ring_dve": _sub(RING, lambda e: e[:2] in ("QK", "WO", "VA", "W1", "W2")),
    "tr_full": TRALL,
    "tr_act": _sub(TRALL, lambda e: e != "MEANp"),
    "tr_dve": _sub(TRALL, lambda e: e == "MEANp"),
    "s_full": GRP, "sub_done": GRP, "exp_done": GRP,
    "pt_full": ATT, "pt_act": ATT, "o_full": ATT, "o_done": ATT,
    "ssq_done": NXT, "ab_done": NXT, "r_done": NXT,
    "norm_in": _per(["NRM"], ["NRM"], ["VARp", "NRM"], ["VARp"], ["VARp"]),
    "norm_exp": _per(["NRM"], ["NRM"], ["VARp", "NRM"], ["VARp"], ["VARp"]),
    "rinv_done": _per(["NRM"], ["NRM"], ["NRM"], [], []),
    "xs_done": _per(["xs0", "xs"], ["xs"], ["xs"], [], []),
    "xv_done": _per(["xv"], ["xv"], ["xv"], [], []),
    "xf_done": _per([], [], ["xf"], ["xf"], ["xf"]),
    "sqx_done": _per([], [], ["sqx"], ["sqx"], ["sqx"]),
    "xc_done": _per([], [], ["xc"], ["xc"], ["xc"]),
    "xn_done": _per([], [], ["xn"], ["xn"], ["xn"]),
    "dve_link": DVE_LINKS,
}


def _len(x):
    return x if isinstance(x, int) else len(x)


def base(sem, kind, s):
    e = {k: _len(EV[sem][k]) for k in KINDS}
    if kind == "pro":
        return 0
    if kind == "first":
        return e["pro"]
    if kind == "mid":
        c = e["pro"] + e["first"] - e["mid"]
        return s * e["mid"] + c
    b = e["pro"] + e["first"] + (STEPS - 2) * e["mid"]
    return b if kind == "last" else b + e["last"]


def val(sem, ev, kind, s):
    return base(sem, kind, s) + (EV[sem][kind].index(ev) + 1)


def prev(sem, ev, kind, s):
    p = {"first": "pro", "mid": "mid", "last": "mid", "tail": "last"}[kind]
    names = EV[sem][p]
    return base(sem, kind, s) - (len(names) - 1 - names.index(ev))


def ring_bank(ev, kind):
    before = {"pro": 0, "first": len(RING["pro"])}
    before["mid"] = before["first"] + len(RING["first"])
    before["last"] = before["mid"]
    before["tail"] = before["last"] + len(RING["last"])
    assert len(RING["mid"]) % 2 == 0
    return (before[kind] + RING[kind].index(ev)) % 2



class Memory:

    def __init__(self, nc, ctx):
        self.nc, self.ctx = nc, ctx

    def sb(self, name, shape, dt=F32):
        return self.ctx.enter_context(self.nc.sbuf_tensor(name, shape, dt))

    def sem(self, name):
        return self.ctx.enter_context(self.nc.semaphore(name))


def mamba_phase(nc, t, banks, ident, xin, XT, ST):
    NI = NB * TILES
    with ExitStack() as ctx:
        m = Memory(nc, ctx)
        sel = m.sb("sel", [DTR + 2 * NST, 2 * NST, P])
        inW = m.sb("inW", [P, 2 * DI])
        dbcW = m.sb("dbcW", [P, DBLK, DTR + 2 * NST])
        outW = m.sb("outW", [P, DBLK, DM])
        dupW = m.sb("dupW", [DTR, DI])
        mvec = m.sb("mvec", [P, MVEC])
        inb, cvb, dupb = mvec[:, 0:4], mvec[:, 4:6], mvec[:, 6:8]
        outb, rmsw = mvec[:, 8:9], mvec[:, 9:10]
        cvw = mvec[:, 10:10 + DBLK * KC].rearrange("p (c k) -> p c k", k=KC)
        Al = mvec[:, 18:18 + DBLK * NST].rearrange("p (c k) -> p c k", k=NST)
        dbcb = m.sb("dbcb", [DTR + 2 * NST, 1])
        Aexp = m.sb("Aexp", [P, DBLK, NST])
        Aneg = m.sb("Aneg", [P, DBLK, NST])
        bst = m.sb("bst", [P, NI, 6])
        st2 = m.sb("st2", [P, NI, 2])
        var = m.sb("var", [P, NI])
        lnv = m.sb("lnv", [P, NI])
        guess = m.sb("guess", [P, NI])
        newt = m.sb("newt", [P, NI])
        rstd = m.sb("rstd", [P, NI])
        msq = m.sb("msq", [P, NI])
        XN = m.sb("XN", [P, NI, DM])
        HN = m.sb("HN", [P, NI, DM])
        HT = m.sb("HT", [P, NB, SEQ])
        x1p = m.sb("x1p", [P, DBLK, KC - 1 + SEQ])
        cv = m.sb("cv", [P, DBLK, SEQ])
        ce = m.sb("ce", [P, DBLK, SEQ])
        x1s = m.sb("x1s", [P, DBLK, SEQ])
        gg = m.sb("gg", [P, DBLK, SEQ])
        gx = m.sb("gx", [P, DBLK, SEQ])
        gs = m.sb("gs", [P, DBLK, SEQ])
        den = m.sb("den", [P, DBLK, SEQ])
        dbc = m.sb("dbc", [DTR + 2 * NST, SEQ])
        sel_r = m.sb("sel_r", [DTR + 2 * NST, 2 * NST, P], F32R)
        dbc_hi = m.sb("dbc_hi", [DTR + 2 * NST, SEQ], F32R)
        dbc_lo = m.sb("dbc_lo", [DTR + 2 * NST, SEQ], F32R)
        dx = m.sb("dx", [P, DBLK, SEQ])
        dn = m.sb("dn", [P, DBLK, SEQ])
        de = m.sb("de", [P, DBLK, SEQ])
        dln = m.sb("dln", [P, DBLK, SEQ])
        delta = m.sb("delta", [P, DBLK, SEQ])
        u = m.sb("u", [P, DBLK, SEQ])
        yg = m.sb("yg", [P, DBLK, SEQ])
        dA = m.sb("dA", [P, 2, DBLK, NP_, SEQ])
        hb = m.sb("hb", [P, 2, DBLK, NP_, SEQ])
        proj, bbk, cbk, ybk = banks[0:2], banks[2:4], banks[4:6], banks[6:8]

        x_in, small_in = m.sem("x_in"), m.sem("small_in")
        dve_link = m.sem("m_dve_link")
        zeroed = m.sem("m_zeroed")
        aexp_done, var_done, guess_done = m.sem("aexp_done"), m.sem("var_done"), m.sem("guess_done")
        norm_done, tp_full, tp_copied = m.sem("norm_done"), m.sem("tp_full"), m.sem("tp_copied")
        proj_full, proj_copied, out_added = m.sem("proj_full"), m.sem("proj_copied"), m.sem("out_added")
        b_full, b_free, c_full = m.sem("b_full"), m.sem("b_free"), m.sem("c_full")
        conv_done, cexp_done, x1_done = m.sem("conv_done"), m.sem("cexp_done"), m.sem("x1_done")
        gexp_done, g_done, dneg_done = m.sem("gexp_done"), m.sem("g_done"), m.sem("dneg_done")
        dexp_done, dln_done, delta_done = m.sem("dexp_done"), m.sem("dln_done"), m.sem("delta_done")
        dA_done, scan_done, hc_done = m.sem("dA_done"), m.sem("scan_done"), m.sem("hc_done")
        y_full, yg_done, split_done = m.sem("y_full"), m.sem("yg_done"), m.sem("split_done")
        PJ, PC = 8, 7
        loads = [
            (ident[:], t["c_ident"]), (inW[:], t["in_W"]),
            (dbcW[:], t["dbc_W"].rearrange("(c p) n -> p c n", p=P)),
            (outW[:], t["out_W"].rearrange("(c p) n -> p c n", p=P)),
            (dupW[:], t["dup_W"]), (mvec[:], t["mamba_vecs"]), (dbcb[:], t["dbc_b"]), (sel[:], t["c_sel"]),
        ]
        SMALL_IN = 16 * len(loads)
        block = ctx.enter_context(nc.Block())

        @block.sync
        def _(sp):
            sp.dma_start(xin[:], t["x"].rearrange("b (i p) n -> p (b i) n", p=P)).then_inc(x_in, 16)
            for dst, src in loads:
                sp.dma_start(dst, src).then_inc(small_in, 16)

        @block.gpsimd
        def _(pool):
            pool.memset(XT[:, :, 0:1], 0.0).then_inc(zeroed, 1)
            pool.memset(x1p[:, :, 0:KC - 1], 0.0).then_inc(zeroed, 1)

        def pe_x1(pe, b):
            for c in range(DBLK):
                if not isinstance(b, int) or b > 0:
                    pe.wait_ge(proj_copied, (b - 1) * PC + 6 + c)
                pe.matmul(proj[1 - c][:, 0:SEQ], inW[:, c * P:(c + 1) * P], HT[:, b, :], start=True, stop=True)\
                  .then_inc(proj_full, 1)

        def pe_batch(pe, b, first, last):
            def done(n, bk):
                pe.wait_ge(proj_copied, b * PC + n)
                return proj[bk]

            for c in range(DBLK):
                if c == 1 and not first:
                    pe.wait_ge(out_added, b)
                    bk = proj[1]
                else:
                    bk = done(2 if c == 0 else 1, c)
                pe.matmul(bk[:, 0:SEQ], inW[:, (DBLK + c) * P:(DBLK + c + 1) * P], HT[:, b, :], start=True, stop=True)\
                  .then_inc(proj_full, 1)
            bk = done(3, 0)
            pe.wait_ge(x1_done, DBLK * b + DBLK)
            for c in range(DBLK):
                mm = pe.matmul(bk[0:DTR + 2 * NST, 0:SEQ], dbcW[:, c, :], x1s[:, c, :], start=c == 0, stop=c == 1)
            mm.then_inc(proj_full, 1)
            bk = done(4, 1)
            pe.wait_ge(proj_copied, b * PC + 5)
            pe.matmul(bk[:, 0:SEQ], dupW[:, 0:P], dbc[0:DTR, :], start=True, stop=True).then_inc(proj_full, 1)
            bk = done(5, 0)
            pe.matmul(bk[:, 0:SEQ], dupW[:, P:2 * P], dbc[0:DTR, :], start=True, stop=True).then_inc(proj_full, 1)
            if not last:
                pe_x1(pe, b + 1)

            pe.wait_ge(split_done, b + 1)

            def rows(which, k, bks, full):
                for j in range(NP_):
                    o = bks[j // 2][:, (j % 2) * SEQ:(j % 2 + 1) * SEQ]
                    pick = sel_r[:, which * NST + k * NP_ + j, :]
                    pe.matmul(o, pick, dbc_hi[:], start=True, stop=False, skip_group_check=True)
                    mm = pe.matmul(o, pick, dbc_lo[:], start=False, stop=True, skip_group_check=True)
                mm.then_inc(full, 1)

            for k in range(PIECES + 1):
                if k < PIECES:
                    if not (first and k == 0):
                        pe.wait_ge(b_free, b * PIECES + k)
                    rows(0, k, bbk, b_full)
                    if not (first and k == 0):
                        pe.wait_ge(hc_done, b * PIECES + k)
                    rows(1, k, cbk, c_full)
                if k > 0:
                    pe.wait_ge(hc_done, b * PIECES + k)
                    if k == 1 and not first:
                        pe.wait_ge(yg_done, DBLK * b)
                    for d in range(DBLK):
                        for j in range(NP_):
                            mm = pe.matmul(ybk[d][:, 0:SEQ], ident[:], hb[:, (k - 1) % 2, d, j, :],
                                           start=k == 1 and j == 0, stop=k == PIECES and j == NP_ - 1)
                    mm.then_inc(y_full, 1)
            bk = done(6 if last else 8, 1)
            pe.wait_ge(yg_done, DBLK * b + DBLK)
            for c in range(DBLK):
                mm = pe.matmul(bk[:, 0:SEQ], outW[:, c, :], yg[:, c, :], start=c == 0, stop=c == 1)
            mm.then_inc(proj_full, 1)

        @block.tensor
        def _(pe):
            pe.wait_ge(small_in, SMALL_IN)
            for n in range(8):
                pe.wait_ge(norm_done, n // 4 + 1)
                if n >= 2:
                    pe.wait_ge(tp_copied, n - 1)
                src = XN if n < 4 else HN
                for j in range(4):
                    mm = pe.transpose(proj[n % 2][:, j * P:(j + 1) * P], src[:, 4 * (n % 4) + j, :], ident[:])
                mm.then_inc(tp_full, 1)
            pe.wait_ge(tp_copied, 8)
            pe_x1(pe, 0)
            pe_batch(pe, 0, True, False)
            with pe.Fori(1, NB - 1) as b:
                pe_batch(pe, b, False, False)
            pe_batch(pe, NB - 1, False, True)

        def act_x1(act, b, first):
            for c in range(DBLK):
                act.wait_ge(proj_full, c + 1 if first else b * PJ + c)
                if not first:
                    act.wait_ge(conv_done, DBLK * b)
                act.activation(x1p[:, c, KC - 1:], proj[1 - c][:, 0:SEQ], ACT.Identity, bias=inb[:, c:c + 1])\
                   .then_inc(proj_copied, 1)

        def act_conv(act, b):
            for c in range(DBLK):
                act.wait_ge(conv_done, DBLK * b + c + 1)
                act.activation(ce[:, c, :], cv[:, c, :], ACT.Exp, scale=-1.0).then_inc(cexp_done, 1)

        def act_batch(act, b, first, last):
            for c in range(DBLK):
                act.wait_ge(proj_full, b * PJ + 2 + c + 1)
                if not first:
                    act.wait_ge(g_done, DBLK * b)
                act.activation(gg[:, c, :], proj[c][:, 0:SEQ], ACT.Identity, bias=inb[:, 2 + c:3 + c])\
                   .then_inc(proj_copied, 1)
            for c in range(DBLK):
                act.wait_ge(proj_copied, b * PC + 3 + c)
                act.activation(gx[:, c, :], gg[:, c, :], ACT.Exp, scale=-1.0).then_inc(gexp_done, 1)
            act.wait_ge(proj_full, b * PJ + 5)
            if not first:
                act.wait_ge(c_full, b * PIECES)
            act.activation(dbc[:], proj[0][0:DTR + 2 * NST, 0:SEQ], ACT.Identity, bias=dbcb[:]).then_inc(proj_copied, 1)
            for c in range(DBLK):
                act.wait_ge(proj_full, b * PJ + 5 + c + 1)
                if not first:
                    act.wait_ge(delta_done, DBLK * b)
                act.activation(dx[:, c, :], proj[(5 + c) % 2][:, 0:SEQ], ACT.Identity, bias=dupb[:, c:c + 1])\
                   .then_inc(proj_copied, 1)
            for c in range(DBLK):
                act.wait_ge(dneg_done, DBLK * b + c + 1)
                act.activation(de[:, c, :], dn[:, c, :], ACT.Exp).then_inc(dexp_done, 1)
            for c in range(DBLK):
                act.wait_ge(dexp_done, DBLK * b + c + 1)
                act.activation(dln[:, c, :], de[:, c, :], ACT.Ln, bias=1.0).then_inc(dln_done, 1)
            for k in range(PIECES):
                for d in range(DBLK):
                    if k == 0:
                        act.wait_ge(delta_done, DBLK * b + d + 1)
                    if not first or k >= 2:
                        act.wait_ge(scan_done, DBLK * PIECES * b + DBLK * (k - 2) + d + 1)
                    for j in range(NP_):
                        n = k * NP_ + j
                        ins = act.activation(dA[:, k % 2, d, j, :], delta[:, d, :], ACT.Exp,
                                             scale=Aneg[:, d, n:n + 1])
                    ins.then_inc(dA_done, 1)
                if k == 1 and not last:
                    act_x1(act, b + 1, False)
            if not last:
                act_conv(act, b + 1)

        @block.scalar
        def _(act):
            act.preload_act_table_set(LN_EXP)
            act.wait_ge(small_in, SMALL_IN)
            act.activation(Aexp[:], Al, ACT.Exp).then_inc(aexp_done, 1)
            for k in range(2):
                act.wait_ge(var_done, k + 1)
                act.activation(lnv[:], var[:], ACT.Ln).then_inc(guess_done, 1)
                act.wait_ge(guess_done, 2 * k + 1)
                act.activation(guess[:], lnv[:], ACT.Exp, scale=-0.5).then_inc(guess_done, 1)
            for n in range(8):
                act.wait_ge(tp_full, n + 1)
                src = proj[n % 2][:].rearrange("p (b t) -> p b t", t=SEQ)
                i = n % 4
                if n < 4:
                    act.activation(XT[:, 2 * i:2 * i + 2, 1:SEQ + 1], src, ACT.Copy).then_inc(tp_copied, 1)
                else:
                    act.activation(HT[:, 2 * i:2 * i + 2, :], src, ACT.Identity, scale=rmsw).then_inc(tp_copied, 1)
            act_x1(act, 0, True)
            act_conv(act, 0)
            act_batch(act, 0, True, False)
            with act.Fori(1, NB - 1) as b:
                act_batch(act, b, False, False)
            act_batch(act, NB - 1, False, True)

        LINKS = (KC - 1) * DBLK + 4 * DBLK + 1 + DBLK + PIECES * DBLK

        def dve_conv(dve, b, first, link):
            for c in range(DBLK):
                dve.wait_ge(proj_copied, b * PC + c + 1)
                if not first:
                    dve.wait_ge(cexp_done, DBLK * b)
                link(dve.tensor_scalar(cv[:, c, :], x1p[:, c, 0:SEQ], cvw[:, c, 0:1], cvb[:, c:c + 1],
                                       ALU.mult, ALU.add))
                for k in range(1, KC):
                    ins = dve.scalar_tensor_tensor(cv[:, c, :], x1p[:, c, k:k + SEQ], cvw[:, c, k:k + 1],
                                                   cv[:, c, :], ALU.mult, ALU.add)
                    if k < KC - 1:
                        link(ins)
                    else:
                        ins.then_inc(conv_done, 1)

        def dve_silu(dve, b, c, src, e, dst, e_done, done, link):
            dve.wait_ge(e_done, DBLK * b + c + 1)
            link(dve.tensor_scalar(den[:, c, :], e[:, c, :], 1.0, None, ALU.add))
            link(dve.reciprocal(den[:, c, :], den[:, c, :]))
            dve.tensor_tensor(dst[:, c, :], src[:, c, :], den[:, c, :], ALU.mult).then_inc(done, 1)

        def dve_batch(dve, b, first, last, before):
            count = [before]

            def link(ins):
                count[0] += 1
                ins.then_inc(dve_link, 1)
                dve.wait_ge(dve_link, b * LINKS + count[0])

            for c in range(DBLK):
                dve_silu(dve, b, c, gg, gx, gs, gexp_done, g_done, link)
            dve.wait_ge(proj_copied, b * PC + 5)
            link(dve.tensor_copy(dbc_hi[:], dbc[:]))
            dve.tensor_tensor(dbc_lo[:], dbc[:], dbc_hi[:].bitcast(F32), ALU.subtract).then_inc(split_done, 1)
            for c in range(DBLK):
                dve.wait_ge(proj_copied, b * PC + 6 + c)
                dve.scalar_tensor_tensor(dn[:, c, :], dx[:, c, :], -1.0, dx[:, c, :], ALU.mult, ALU.min)\
                   .then_inc(dneg_done, 1)
            for c in range(DBLK):
                dve.wait_ge(dln_done, DBLK * b + c + 1)
                if not first:
                    dve.wait_ge(dA_done, DBLK * PIECES * b)
                dve.scalar_tensor_tensor(delta[:, c, :], dx[:, c, :], 0.0, dln[:, c, :], ALU.max, ALU.add)\
                   .then_inc(delta_done, 1)
                dve.wait_ge(delta_done, DBLK * b + c + 1)
                link(dve.tensor_tensor(u[:, c, :], delta[:, c, :], x1s[:, c, :], ALU.mult))
            for k in range(PIECES):
                n = b * PIECES + k
                dve.wait_ge(b_full, n + 1)
                if not first or k >= 2:
                    dve.wait_ge(y_full, n - 1)
                for d in range(DBLK):
                    for j in range(2):
                        ins = dve.tensor_tensor(hb[:, k % 2, d, 2 * j:2 * j + 2, :],
                                                bbk[j][:].rearrange("p (j t) -> p j t", t=SEQ),
                                                u[:, d:d + 1, :].broadcast_to([P, 2, SEQ]), ALU.mult)
                ins.then_inc(b_free, 1)
                for d in range(DBLK):
                    dve.wait_ge(dA_done, DBLK * n + d + 1)
                    link(dve.memset(dA[:, k % 2, d, :, 0:1], 0.0))
                for d in range(DBLK):
                    dve.wait_ge(b_free, n + 1)
                    flat = hb[:, k % 2, d].rearrange("p j t -> p (j t)")
                    dve.tensor_tensor_scan(flat, dA[:, k % 2, d].rearrange("p j t -> p (j t)"), flat, 0.0,
                                           ALU.mult, ALU.add).then_inc(scan_done, 1)
                dve.wait_ge(c_full, n + 1)
                for d in range(DBLK):
                    dve.wait_ge(scan_done, DBLK * n + d + 1)
                    for j in range(2):
                        h = hb[:, k % 2, d, 2 * j:2 * j + 2, :]
                        ins = dve.tensor_tensor(h, cbk[j][:].rearrange("p (j t) -> p j t", t=SEQ), h, ALU.mult)
                ins.then_inc(hc_done, 1)
            if not last:
                dve_conv(dve, b + 1, False, link)
                dve_silu(dve, b + 1, 0, cv, ce, x1s, cexp_done, x1_done, link)
            dve.wait_ge(y_full, (b + 1) * PIECES)
            if not first:
                dve.wait_ge(proj_full, b * PJ + 2)
            for c in range(DBLK):
                dve.wait_ge(g_done, DBLK * b + c + 1)
                dve.tensor_tensor(yg[:, c, :], ybk[c][:, 0:SEQ], gs[:, c, :], ALU.mult).then_inc(yg_done, 1)
            if not last:
                dve_silu(dve, b + 1, 1, cv, ce, x1s, cexp_done, x1_done, link)
            dve.wait_ge(proj_full, b * PJ + (8 if last else 10))
            dve.scalar_tensor_tensor(ST[:, b, :], proj[1][:, 0:SEQ], outb, XT[:, b, 1:SEQ + 1], ALU.add, ALU.add)\
               .then_inc(out_added, 1)
            return count[0] - before

        @block.vector
        def _(dve):
            count = [0]

            def link(ins):
                count[0] += 1
                ins.then_inc(dve_link, 1)
                dve.wait_ge(dve_link, count[0])

            def row(ap):
                return ap.rearrange("p (i o) -> p i o", o=1).broadcast_to([P, NI, DM])

            def rsqrt(k):
                dve.wait_ge(guess_done, 2 * k + 2)
                link(dve.tensor_tensor(newt[:], guess[:], guess[:], ALU.mult))
                link(dve.scalar_tensor_tensor(newt[:], newt[:], -0.5, var[:], ALU.mult, ALU.mult))
                link(dve.scalar_tensor_tensor(rstd[:], newt[:], 1.5, guess[:], ALU.add, ALU.mult))

            dve.wait_ge(x_in, 16)
            for i in range(NI):
                ins = dve.bn_stats(bst[:, i, :], xin[:, i, :])
            link(ins)
            for i in range(NI):
                ins = dve.bn_aggr(st2[:, i, :], bst[:, i, :])
            link(ins)
            dve.tensor_scalar(var[:], st2[:, :, 1], 1e-5, None, ALU.add).then_inc(var_done, 1)
            link(dve.tensor_copy(msq[:], st2[:, :, 0]))
            link(dve.tensor_tensor(XN[:], xin[:], row(msq[:]), ALU.subtract))
            dve.wait_ge(var_done, 1)
            rsqrt(0)
            dve.tensor_tensor(XN[:], XN[:], row(rstd[:]), ALU.mult).then_inc(norm_done, 1)
            dve.wait_ge(norm_done, 1)
            link(dve.tensor_tensor(HN[:], XN[:], XN[:], ALU.mult))
            link(dve.reduce_sum(msq[:], HN[:], AX_X))
            dve.tensor_scalar(var[:], msq[:], 1.0 / DM, 1e-6, ALU.mult, ALU.add).then_inc(var_done, 1)
            dve.wait_ge(var_done, 2)
            rsqrt(1)
            dve.tensor_tensor(HN[:], XN[:], row(rstd[:]), ALU.mult).then_inc(norm_done, 1)
            dve.wait_ge(aexp_done, 1)
            link(dve.tensor_copy(sel_r[:], sel[:]))
            link(dve.tensor_scalar(Aneg[:], Aexp[:], -1.0, None, ALU.mult))
            dve.wait_ge(zeroed, 2)
            dve_conv(dve, 0, True, link)
            for c in range(DBLK):
                dve_silu(dve, 0, c, cv, ce, x1s, cexp_done, x1_done, link)
            before = count[0]
            got = dve_batch(dve, 0, True, False, before)
            with dve.Fori(1, NB - 1) as b:
                dve_batch(dve, b, False, False, before)
            dve_batch(dve, NB - 1, False, True, before)
            assert got == LINKS, (got, LINKS)


def transformer_phase(nc, t, banks, scores_banks, ident, XT):
    with ExitStack() as ctx:
        m = Memory(nc, ctx)
        S = {name: m.sem(name) for name in EV}
        identb = m.sb("identb", [P, P], BF16)
        maskb = m.sb("maskb", [P, TILES * 2 * 2 * WIN], BF16)
        rot = m.sb("rot", [P, 2, TILES, 2, DH])
        mean = m.sb("mean", [P, P])
        vecs = m.sb("vecs", [P, DEPTH, NVEC])
        qks = m.sb("qks", [P, DEPTH, 2, DH])
        wqkv = m.sb("wqkv", [P, 2, 3 * INNER])
        wo = m.sb("wo", [P, 2 * GROUPS, DM])
        w1 = m.sb("w1", [P, 2 * FFI])
        w2 = m.sb("w2", [P, 3, DM])
        xs = m.sb("xs", [P, SEQ])
        xv = m.sb("xv", [P, SEQ])
        rt = m.sb("rt", [P, 2, TILES, 2, DH])
        sq = m.sb("sq", [P, 2, 512])
        qc = m.sb("qc", [P, 2, 512])
        qn = m.sb("qn", [P, 2, 512])
        AB = m.sb("AB", [P, 8, 512])
        ssq = m.sb("ssq", [P, 64])
        ssc = m.sb("ssc", [P, 64])
        lnq = m.sb("lnq", [P, 64])
        rs0 = m.sb("rs0", [P, 64])
        rs1 = m.sb("rs1", [P, 64])
        rinv = m.sb("rinv", [P, 64])
        qT = m.sb("qT", [P, 2, 2, SEQ])
        kT = m.sb("kT", [P, 2, 2, WIN + SEQ])
        V = m.sb("V", [P, TILES, HEADS, VH])
        mx = m.sb("mx", [P, 8])
        Pc = m.sb("Pc", [P, 2, 8, 2 * WIN])
        Pd = m.sb("Pd", [P, 2, 8, P])
        Pp = m.sb("Pp", [WIN, 2, GH, P])
        PT = m.sb("PT", [P, TILES, GH, P])
        PTp = m.sb("PTp", [P, GH, WIN])
        rden = m.sb("rden", [P, TILES, GH])
        On = m.sb("On", [P, TILES, INNER])
        OT = m.sb("OT", [P, 2 * GROUPS, SEQ])
        cur = m.sb("cur", [P, NVEC])
        xf = m.sb("xf", [P, SEQ])
        xc = m.sb("xc", [P, SEQ])
        sqx = m.sb("sqx", [P, SEQ])
        var = m.sb("fvar", [P, SEQ])
        lnx = m.sb("lnx", [P, SEQ])
        y0 = m.sb("y0", [P, SEQ])
        y1 = m.sb("y1", [P, SEQ])
        xy = m.sb("xy", [P, SEQ])
        xn = m.sb("xn", [P, SEQ])
        ge = m.sb("ge", [P, 3, SEQ])
        hh = m.sb("hh", [P, 3, SEQ])
        ebias = m.sb("ebias", [P, 1])
        ring, trb, sbk, ptb, ob = banks[0:2], banks[2], scores_banks, banks[5], banks[6:8]
        const_in, wqkv_in = m.sem("const_in"), m.sem("wqkv_in")
        wo_in, w1_in, w2_in = m.sem("wo_in"), m.sem("w1_in"), m.sem("w2_in")
        pool_set, mask_set, act_link = m.sem("pool_set"), m.sem("mask_set"), m.sem("act_link")
        POOL_SET = 7
        loads = [(xy[:], t["c_mask"]), (rot[:], t["c_rot"]),
                 (vecs[:], t["layer_vecs"]),
                 (qks[:, :, 0, :], t["q_scale"].partition_broadcast(P)),
                 (qks[:, :, 1, :], t["k_scale"].partition_broadcast(P))]
        CONST_IN = 16 * len(loads)

        block = ctx.enter_context(nc.Block())

        @block.sync
        def _(sp):
            def load_qkv(l, buf):
                w = t["Wqkv"][l]
                dst = wqkv[:, buf, 0:2 * INNER].rearrange("p (g c n) -> p g c n", g=GROUPS, c=2)
                for c in range(2):
                    sp.dma_start(dst[:, :, c, :], w[:, c * INNER:(c + 1) * INNER]
                                 .rearrange("p (g n) -> p g n", g=GROUPS)).then_inc(wqkv_in, 16)
                sp.dma_start(wqkv[:, buf, 2 * INNER:], w[:, 2 * INNER:]).then_inc(wqkv_in, 16)

            def load_wo(l):
                sp.dma_start(wo[:], t["Wo"][l].rearrange("(c p) n -> p c n", p=P)).then_inc(wo_in, 16)

            def load_ff(l):
                sp.dma_start(w1[:], t["W1"][l]).then_inc(w1_in, 16)
                sp.dma_start(w2[:, 0:2, :], t["W2"][l][0:2 * P, :].rearrange("(c p) n -> p c n", p=P))\
                  .then_inc(w2_in, 16)
                sp.dma_start(w2[0:FFI - 2 * P, 2, :], t["W2"][l][2 * P:FFI, :]).then_inc(w2_in, 16)

            load_qkv(0, 0)
            for dst, src in loads:
                sp.dma_start(dst, src).then_inc(const_in, 16)
            load_wo(0)
            load_ff(0)
            sp.wait_ge(wqkv_in, 48)
            load_qkv(1, 1)

            def reload(l):
                sp.wait_ge(S["ring_full"], val("ring_full", "WOp", "mid", l * NB))
                sp.wait_ge(wo_in, l * 16)
                load_wo(l)
                sp.wait_ge(S["ring_full"], val("ring_full", "W2p", "mid", l * NB))
                load_ff(l)

            for l in range(1, DEPTH):
                reload(l)
                if l < DEPTH - 1:
                    sp.wait_ge(wqkv_in, (l + 1) * 48)
                    load_qkv(l + 1, (l + 1) % 2)

        def pe_step(pe, kind, s):
            att, nxt, ffp = kind in ("first", "mid", "last"), kind in ("pro", "first", "mid"), kind in ("mid", "last", "tail")
            if kind == "pro":
                layer_n, layer_p = 0, None
            else:
                layer_n, layer_p = (s + 1) // NB, (s - 1) // NB
            buf = layer_n % 2

            def ring_unit(ev):
                names = RING[kind]
                i = names.index(ev)
                if i >= 2:
                    old, f = names[i - 2], val
                elif kind != "pro":
                    p = {"first": "pro", "mid": "mid", "last": "mid", "tail": "last"}[kind]
                    old, f = RING[p][i - 2], prev
                else:
                    return ring[ring_bank(ev, kind)]
                for q in ("ring_act", "ring_dve"):
                    if old in EV[q][kind if f is val else p]:
                        pe.wait_ge(S[q], f(q, old, kind, s))
                return ring[ring_bank(ev, kind)]

            def qk(g, tl):
                bk = ring_unit(f"QK{g}{tl}")
                if (g, tl) == (0, 0):
                    pe.wait_ge(S["xs_done"], val("xs_done", "xs0", kind, s) if kind == "pro" else base("xs_done", kind, s))
                    pe.wait_ge(wqkv_in, layer_n * 48 + 48)
                pe.matmul(bk[:], xs[:, tl * P:(tl + 1) * P], wqkv[:, buf, g * 512:(g + 1) * 512], start=True, stop=True)\
                  .then_inc(S["ring_full"], 1)

            def v(n):
                bk = ring_unit(f"V{n}")
                tl, hf = n // 2, n % 2
                if n == 0:
                    pe.wait_ge(S["xv_done"], val("xv_done", "xv", kind, s))
                pe.matmul(bk[:], xv[:, tl * P:(tl + 1) * P],
                          wqkv[:, buf, 2 * INNER + hf * 512:2 * INNER + (hf + 1) * 512], start=True, stop=True)\
                  .then_inc(S["ring_full"], 1)

            def tr(g, tl):
                i = EV["tr_full"][kind].index(f"{g}{tl}")
                if i == 0 and kind != "first":
                    pe.wait_ge(S["tr_act"], base("tr_act", kind, s))
                elif i > 0:
                    old = EV["tr_full"][kind][i - 1]
                    q = "tr_dve" if old == "MEANp" else "tr_act"
                    pe.wait_ge(S[q], val(q, old, kind, s))
                pe.wait_ge(S["r_done"], prev("r_done", f"QK{g}{tl}", kind, s))
                for c in range(4):
                    mm = pe.transpose(trb[:, c * P:(c + 1) * P], AB[:, 2 * g + tl, c * P:(c + 1) * P], ident[:])
                mm.then_inc(S["tr_full"], 1)

            def scores(g):
                pe.wait_ge(S["tr_act"], val("tr_act", f"{g}1", kind, s))
                if g > 0:
                    pe.wait_ge(S["sub_done"], val("sub_done", f"{g - 1}", kind, s))
                elif kind != "first":
                    pe.wait_ge(S["sub_done"], base("sub_done", kind, s))
                for odd in range(2):
                    pe.matmul(sbk[:, odd, 0:2 * TILES * 2 * WIN], identb[:], maskb[:], start=True, stop=False,
                              skip_group_check=True)
                for tl in range(TILES):
                    for c in range(2):
                        for w in range(4):
                            tok, col = tl * P + w * WIN, (2 * tl + c) * 2 * WIN
                            for odd in range(2):
                                p0 = DH * odd
                                mm = pe.matmul(sbk[w * WIN:(w + 1) * WIN, odd, col:col + 2 * WIN],
                                               qT[p0:p0 + DH, g % 2, c, tok:tok + WIN],
                                               kT[p0:p0 + DH, g % 2, c, tok:tok + 2 * WIN],
                                               start=False, stop=True, skip_group_check=True)
                mm.then_inc(S["s_full"], 1)

            def ptr(g, tl):
                if tl == 0:
                    pe.wait_ge(S["exp_done"], val("exp_done", f"{g}", kind, s))
                if tl == 1:
                    pe.wait_ge(S["pt_act"], val("pt_act", f"{g}0", kind, s))
                elif g > 0:
                    pe.wait_ge(S["pt_act"], val("pt_act", f"{g - 1}1", kind, s))
                elif kind != "first":
                    pe.wait_ge(S["pt_act"], base("pt_act", kind, s))
                if tl == 1:
                    if g > 0:
                        pe.wait_ge(S["o_done"], val("o_done", f"{g - 1}1", kind, s))
                    elif kind != "first":
                        pe.wait_ge(S["o_done"], base("o_done", kind, s))
                for h in range(GH):
                    mm = pe.transpose(ptb[:, h * P:(h + 1) * P], Pd[:, g % 2, 4 * (h // 2) + 2 * tl + h % 2, :],
                                      ident[:])
                if tl == 1:
                    for h in range(GH):
                        mm = pe.transpose(ob[1][:, 3 * P + h * WIN:3 * P + (h + 1) * WIN], Pp[:, g % 2, h, :],
                                          ident[0:WIN, 0:WIN])
                mm.then_inc(S["pt_full"], 1)

            def ov(g, tl):
                pe.wait_ge(S["pt_act"], val("pt_act", f"{g}{tl}", kind, s))
                if tl == 0:
                    if g > 0:
                        pe.wait_ge(S["o_done"], val("o_done", f"{g - 1}0", kind, s))
                    else:
                        pe.wait_ge(S["ring_act"], prev("ring_act", "V3", kind, s))
                for h in range(GH):
                    o = ob[tl][:, h * VH:(h + 1) * VH]
                    at = 2 * (h % 2) + h // 2
                    mm = pe.matmul(o, PT[:, tl, at, :], V[:, tl, g * GH + h, :], start=True, stop=tl == 0,
                                   skip_group_check=True)
                    if tl == 1:
                        mm = pe.matmul(ob[1][0:WIN, h * VH:(h + 1) * VH], PTp[:, at, :], V[:, 0, g * GH + h, :],
                                       start=False, stop=True, skip_group_check=True)
                mm.then_inc(S["o_full"], 1)

            def ot(g, ev):
                bk = ring_unit(ev)
                f = prev if ev.endswith("p") else val
                pe.wait_ge(S["o_done"], f("o_done", f"{g}1", kind, s))
                for c in range(2):
                    for tl in range(TILES):
                        mm = pe.transpose(bk[:, (2 * c + tl) * P:(2 * c + tl + 1) * P],
                                          On[:, tl, (2 * g + c) * P:(2 * g + c + 1) * P], ident[:])
                mm.then_inc(S["ring_full"], 1)

            def w_out():
                bk = ring_unit("WOp")
                pe.wait_ge(S["ring_act"], val("ring_act", "OT3p", kind, s))
                pe.wait_ge(wo_in, layer_p * 16 + 16)
                for k in range(2 * GROUPS):
                    mm = pe.matmul(bk[:, 0:SEQ], wo[:, k, :], OT[:, k, :], start=k == 0, stop=k == 2 * GROUPS - 1)
                mm.then_inc(S["ring_full"], 1)

            def mean_x():
                if kind == "tail":
                    pe.wait_ge(S["tr_act"], base("tr_act", kind, s))
                else:
                    pe.wait_ge(S["tr_act"], val("tr_act", "11", kind, s))
                pe.wait_ge(S["xf_done"], val("xf_done", "xf", kind, s))
                pe.matmul(trb[:, 0:SEQ], mean[:], xf[:], start=True, stop=True).then_inc(S["tr_full"], 1)

            def var_x():
                bk = ring_unit("VARp")
                pe.wait_ge(S["sqx_done"], val("sqx_done", "sqx", kind, s))
                pe.matmul(bk[:, 0:SEQ], mean[:], sqx[:], start=True, stop=True).then_inc(S["ring_full"], 1)

            def w_1():
                for c, (f0, n) in enumerate(FFC):
                    bk = ring_unit(f"W1{'abc'[c]}p")
                    if c == 0:
                        pe.wait_ge(S["xn_done"], val("xn_done", "xn", kind, s))
                        pe.wait_ge(w1_in, layer_p * 16 + 16)
                    for h in range(2):
                        mm = pe.matmul(bk[0:n, h * SEQ:(h + 1) * SEQ], w1[:, h * FFI + f0:h * FFI + f0 + n], xn[:],
                                       start=True, stop=True, skip_group_check=True)
                    mm.then_inc(S["ring_full"], 1)

            def w_2():
                bk = ring_unit("W2p")
                pe.wait_ge(S["ring_dve"], val("ring_dve", "W1cp", kind, s))
                pe.wait_ge(w2_in, layer_p * 32 + 32)
                for c, (f0, n) in enumerate(FFC):
                    mm = pe.matmul(bk[:, 0:SEQ], w2[0:n, c, :], hh[0:n, c, :], start=c == 0, stop=c == 2)
                mm.then_inc(S["ring_full"], 1)

            if kind == "pro":
                for g in range(GROUPS):
                    qk(g, 0)
                    qk(g, 1)
                for n in range(4):
                    v(n)
                return
            if kind == "tail":
                ot(3, "OT3p")
                w_out()
                mean_x()
                var_x()
                w_1()
                w_2()
                return
            for k in range(5):
                if k == 0 and ffp:
                    ot(3, "OT3p")
                if k < 4:
                    if k != 2:
                        tr(k, 0)
                    if nxt and k < 3:
                        qk(k, 0)
                    if ffp and k == 3:
                        w_2()
                    tr(k, 1)
                    if nxt and k < 3:
                        qk(k, 1)
                elif nxt:
                    qk(3, 0)
                    ptr(3, 0)
                    qk(3, 1)
                if k == 0:
                    scores(0)
                if ffp and k < 2:
                    (w_out, mean_x)[k]()
                if k > 0 and not (k == 4 and nxt):
                    ptr(k - 1, 0)
                if 0 < k < 4:
                    scores(k)
                if ffp and k == 2:
                    w_1()
                if k > 0 and k < 4:
                    ptr(k - 1, 1)
                    ov(k - 1, 0)
                    if ffp and k == 1:
                        var_x()
                    if k == 1:
                        tr(2, 0)
                    ov(k - 1, 1)
                    if k >= 2:
                        ot(k - 2, f"OT{k - 2}")
            ptr(3, 1)
            ov(3, 0)
            ot(2, "OT2")
            ov(3, 1)
            if nxt:
                for n in range(4):
                    v(n)

        def act_step(act, kind, s):
            nxt, ffp = kind in ("pro", "first", "mid"), kind in ("mid", "last", "tail")
            b_next = 0 if kind == "pro" else (s + 1) % NB
            b_prev = None if kind in ("pro", "first") else (s - 1) % NB

            def ring_in(ev):
                act.wait_ge(S["ring_full"], val("ring_full", ev, kind, s))
                return ring[ring_bank(ev, kind)]

            def shifted(dst, b, done):
                act.activation(dst[0:DM // 2, :], XT[0:DM // 2, b, 1:SEQ + 1], ACT.Copy)
                act.activation(dst[DM // 2:, :], XT[DM // 2:, b, 0:SEQ], ACT.Copy).then_inc(done, 1)

            def make_xs():
                act.wait_ge(S["ring_full"], val("ring_full", "QK31", kind, s))
                if kind == "mid":
                    act.wait_ge(S["ring_dve"], base("ring_dve", kind, s))
                shifted(xs, 1 if kind == "pro" else (s + 2) % NB, S["xs_done"])

            def make_xv():
                if kind != "pro":
                    act.wait_ge(S["ring_full"], prev("ring_full", "V3", kind, s))
                if kind == "mid":
                    act.wait_ge(S["ring_dve"], base("ring_dve", kind, s))
                shifted(xv, b_next, S["xv_done"])

            def make_xf():
                act.wait_ge(S["ring_dve"], val("ring_dve", "WOp", kind, s))
                shifted(xf, b_prev, S["xf_done"])

            def square_qk(g, tl):
                bk = ring_in(f"QK{g}{tl}")
                i = 2 * g + tl
                if i >= 2:
                    act.wait_ge(S["ssq_done"], val("ssq_done", QK[i - 2], kind, s))
                elif kind != "pro":
                    act.wait_ge(S["ssq_done"], prev("ssq_done", QK[6 + i], kind, s))
                act.activation(sq[:, tl, :], bk[:], ACT.Square).then_inc(S["ring_act"], 1)

            def copy_tr(g, tl):
                act.wait_ge(S["tr_full"], val("tr_full", f"{g}{tl}", kind, s))
                if g >= 2:
                    act.wait_ge(S["s_full"], val("s_full", f"{g - 2}", kind, s))
                elif kind != "first":
                    act.wait_ge(S["s_full"], prev("s_full", f"{g + 2}", kind, s))
                src = trb[:].rearrange("p (c t) -> p c t", t=P)
                act.activation(qT[:, g % 2, :, tl * P:(tl + 1) * P], src[:, 0:2, :], ACT.Copy)
                act.activation(kT[:, g % 2, :, WIN + tl * P:WIN + (tl + 1) * P], src[:, 2:4, :], ACT.Copy)\
                   .then_inc(S["tr_act"], 1)

            def exp_p(g):
                act.wait_ge(S["sub_done"], val("sub_done", f"{g}", kind, s))
                if g >= 2:
                    act.wait_ge(S["pt_full"], val("pt_full", f"{g - 2}1", kind, s))
                elif kind != "first":
                    act.wait_ge(S["pt_full"], prev("pt_full", f"{g + 2}1", kind, s))
                p = g % 2
                act.activation(Pd[0:WIN, p, :, 0:WIN], Pc[0:WIN, p, :, WIN:], ACT.Exp, scale=QK_SCALE)
                act.activation(Pp[:, p, :, P - WIN:].rearrange("p (o c) j -> p o c j", o=2),
                               Pc[0:WIN, p, :, 0:WIN].rearrange("p (o t c) j -> p o t c j", o=2, t=2)[:, :, 1],
                               ACT.Exp, scale=QK_SCALE)
                for w in range(1, 4):
                    ins = act.activation(Pd[w * WIN:(w + 1) * WIN, p, :, (w - 1) * WIN:(w + 1) * WIN],
                                         Pc[w * WIN:(w + 1) * WIN, p, :, :], ACT.Exp, scale=QK_SCALE)
                ins.then_inc(S["exp_done"], 1)

            def copy_pt(g, tl):
                act.wait_ge(S["pt_full"], val("pt_full", f"{g}{tl}", kind, s))
                if g > 0:
                    act.wait_ge(S["o_full"], val("o_full", f"{g - 1}{tl}", kind, s))
                elif kind != "first":
                    act.wait_ge(S["o_full"], prev("o_full", f"3{tl}", kind, s))
                if tl == 1:
                    act.activation(PTp[:], ob[1][:, 3 * P:4 * P].rearrange("p (h i) -> p h i", h=GH), ACT.Copy)
                act.activation(PT[:, tl, :, :], ptb.rearrange("p (h i) -> p h i", h=GH), ACT.Copy)\
                   .then_inc(S["pt_act"], 1)

            def copy_ot(g, ev):
                bk = ring_in(ev)
                if ev == "OT0" and ffp:
                    act.wait_ge(S["ring_full"], val("ring_full", "WOp", kind, s))
                act.activation(OT[:, 2 * g:2 * g + 2, :], bk[:].rearrange("p (c t) -> p c t", c=2), ACT.Copy)\
                   .then_inc(S["ring_act"], 1)

            def copy_v(n):
                bk = ring_in(f"V{n}")
                tl, hf = n // 2, n % 2
                if kind != "pro" and n == 0:
                    act.wait_ge(S["o_full"], val("o_full", "31", kind, s))
                act.activation(V[:, tl, 8 * hf:8 * hf + 8, 0:DH], bk[:].rearrange("p (h d) -> p h d", h=8), ACT.Copy)\
                   .then_inc(S["ring_act"], 1)

            def guess(ev, src, ln, dst, **kw):
                act.wait_ge(S["norm_in"], val("norm_in", ev, kind, s))
                act.activation(ln[:], src[:], ACT.Ln, **kw).then_inc(act_link, 1)
                n = {"pro": 0, "first": 1, "mid": 2, "last": 2, "tail": 2}[kind]
                order = 1 if ev == "VARp" or kind in ("pro", "first") else 2
                before = {"pro": 0, "first": 1, "last": 2 + 2 * (STEPS - 2), "tail": 3 + 2 * (STEPS - 2)}
                start = 2 * s if kind == "mid" else before[kind]
                act.wait_ge(act_link, start + order)
                if ev == "NRM":
                    act.activation(dst[:], ln[:], ACT.Exp, scale=-0.5, bias=ebias[:]).then_inc(S["norm_exp"], 1)
                else:
                    act.activation(dst[:], ln[:], ACT.Exp, scale=-0.5).then_inc(S["norm_exp"], 1)

            def square_x():
                act.wait_ge(S["xc_done"], val("xc_done", "xc", kind, s))
                act.activation(sqx[:], xc[:], ACT.Square).then_inc(S["sqx_done"], 1)

            def gelu():
                for c, (f0, n) in enumerate(FFC):
                    bk = ring_in(f"W1{'abc'[c]}p")
                    act.activation(ge[0:n, c, :], bk[0:n, SEQ:], ACT.Gelu, bias=cur[0:n, 6 + c:7 + c])\
                       .then_inc(S["ring_act"], 1)

            if kind == "pro":
                shifted(xs, 0, S["xs_done"])
                make_xv()
                for g in range(GROUPS):
                    square_qk(g, 0)
                    square_qk(g, 1)
                make_xs()
                for n in range(4):
                    copy_v(n)
                guess("NRM", ssc, lnq, rs0, scale=2.0 ** 16)
                return
            if kind == "tail":
                copy_ot(3, "OT3p")
                make_xf()
                square_x()
                guess("VARp", var, lnx, y0)
                gelu()
                return
            for k in range(5):
                if k == 4 and nxt:
                    make_xv()
                if k == 0 and ffp:
                    copy_ot(3, "OT3p")
                if k < 4:
                    if k < 2:
                        copy_tr(k, 0)
                    if ffp and k == 1:
                        make_xf()
                    if nxt and k < 3:
                        square_qk(k, 0)
                    copy_tr(k, 1)
                    if nxt and k < 3:
                        square_qk(k, 1)
                elif nxt:
                    square_qk(3, 0)
                    copy_pt(3, 0)
                    square_qk(3, 1)
                if k == 0:
                    exp_p(0)
                if k > 0:
                    if not (k == 4 and nxt):
                        copy_pt(k - 1, 0)
                    if ffp and k == 2:
                        gelu()
                    if ffp and k == 1:
                        square_x()
                    copy_pt(k - 1, 1)
                    if ffp and k == 2:
                        act.preload_act_table_set(LN_EXP)
                if ffp and k == 1:
                    guess("VARp", var, lnx, y0)
                if k == 1:
                    copy_tr(2, 0)
                if 0 < k < 4:
                    exp_p(k)
                if k == 2:
                    copy_tr(3, 0)
                if 2 <= k < 4:
                    copy_ot(k - 2, f"OT{k - 2}")
            copy_ot(2, "OT2")
            if nxt:
                guess("NRM", ssc, lnq, rs0, scale=2.0 ** 16)
                make_xs()
                for n in range(4):
                    copy_v(n)

        def dve_step(dve, kind, s):
            nxt, ffp = kind in ("pro", "first", "mid"), kind in ("mid", "last", "tail")
            layer_n = 0 if kind == "pro" else (s + 1) // NB
            layer_p = None if kind in ("pro", "first") else (s - 1) // NB
            b_prev = None if kind in ("pro", "first") else (s - 1) % NB
            links = [0]

            def link(ins):
                links[0] += 1
                ins.then_inc(S["dve_link"], 1)
                dve.wait_ge(S["dve_link"], base("dve_link", kind, s) + links[0])

            def ring_in(ev):
                dve.wait_ge(S["ring_full"], val("ring_full", ev, kind, s))
                return ring[ring_bank(ev, kind)]

            def tables():
                for z in range(2):
                    ins = dve.tensor_tensor(rt[:, z].rearrange("p t c d -> p t (c d)"),
                                            rot[:, z].rearrange("p t c d -> p t (c d)"),
                                            qks[:, layer_n, :, :].rearrange("p (o c) d -> p o (c d)", o=1)
                                            .broadcast_to([P, TILES, 2 * DH]), ALU.mult)
                link(ins)

            def qk(g, tl):
                i = 2 * g + tl
                ev = QK[i]
                dve.wait_ge(S["ring_act"], val("ring_act", ev, kind, s))
                bk = ring_in(ev)
                if i >= 2:
                    dve.wait_ge(S["ab_done"], val("ab_done", QK[i - 2], kind, s))
                elif kind != "pro":
                    dve.wait_ge(S["ab_done"], prev("ab_done", QK[6 + i], kind, s))
                src = bk[:].rearrange("p (c h d) -> p c h d", c=2, h=GH)
                for z, dst in ((0, qc), (1, qn)):
                    tb = rt[:, z, tl].rearrange("p c (o d) -> p c o d", o=1).broadcast_to([P, 2, GH, DH])
                    ins = dve.tensor_tensor(dst[:, tl, :].rearrange("p (c h d) -> p c h d", c=2, h=GH), src, tb,
                                            ALU.mult)
                ins.then_inc(S["ring_dve"], 1)
                dve.reduce_sum(ssq[:, 8 * i:8 * i + 8], sq[:, tl, :].rearrange("p (h d) -> p h d", d=DH), AX_X)\
                   .then_inc(S["ssq_done"], 1)

            def softmax(g):
                dve.wait_ge(S["s_full"], val("s_full", f"{g}", kind, s))
                src = sbk[:, :, 0:4 * 2 * WIN].rearrange("p o (h j) -> p o h j", h=4)
                dst = Pc[:, g % 2, :, :].rearrange("p (o h) j -> p o h j", o=2)
                link(dve.reduce_max(mx[:].rearrange("p (o h) -> p o h", o=2), src, AX_X))
                if g >= 2:
                    dve.wait_ge(S["exp_done"], val("exp_done", f"{g - 2}", kind, s))
                elif kind != "first":
                    dve.wait_ge(S["exp_done"], prev("exp_done", f"{g + 2}", kind, s))
                dve.tensor_tensor(dst, src, mx[:].rearrange("p (o h e) -> p o h e", o=2, e=1)
                                  .broadcast_to([P, 2, 4, 2 * WIN]),
                                  ALU.subtract).then_inc(S["sub_done"], 1)

            def norm_o(g, tl):
                dve.wait_ge(S["o_full"], val("o_full", f"{g}{tl}", kind, s))
                o = ob[tl][:, 0:GH * VH].rearrange("p (h d) -> p h d", h=GH)
                link(dve.reciprocal(rden[:, tl, :], o[:, :, DH]))
                if g == 0 and ffp and tl == 0:
                    dve.wait_ge(S["ring_full"], val("ring_full", "OT3p", kind, s))
                dve.tensor_tensor(On[:, tl, g * GH * DH:(g + 1) * GH * DH].rearrange("p (h d) -> p h d", h=GH),
                                  o[:, :, 0:DH],
                                  rden[:, tl, :].rearrange("p (h o) -> p h o", o=1).broadcast_to([P, GH, DH]), ALU.mult)\
                   .then_inc(S["o_done"], 1)

            def newton(ev, v, y, tmp, out, done):
                dve.wait_ge(S["norm_exp"], val("norm_exp", ev, kind, s))
                link(dve.tensor_tensor(tmp[:], y[:], y[:], ALU.mult))
                link(dve.scalar_tensor_tensor(tmp[:], tmp[:], -0.5, v[:], ALU.mult, ALU.mult))
                ins = dve.scalar_tensor_tensor(out[:], tmp[:], 1.5, y[:], ALU.add, ALU.mult)
                if done is None:
                    link(ins)
                else:
                    ins.then_inc(done, 1)

            def norm_qk_in():
                dve.wait_ge(S["ssq_done"], val("ssq_done", "QK31", kind, s))
                dve.tensor_scalar(ssc[:], ssq[:], 1e-24, None, ALU.max).then_inc(S["norm_in"], 1)

            def norm_qk():
                if kind != "pro":
                    dve.wait_ge(S["r_done"], base("r_done", kind, s))
                newton("NRM", ssc, rs0, rs1, rinv, S["rinv_done"])

            def res_attention():
                bk = ring_in("WOp")
                x = XT[:, b_prev, 1:SEQ + 1]
                dve.tensor_tensor(x, bk[:, 0:SEQ], x, ALU.add).then_inc(S["ring_dve"], 1)

            def center():
                dve.wait_ge(S["tr_full"], val("tr_full", "MEANp", kind, s))
                dve.tensor_tensor(xc[:], xf[:], trb[:, 0:SEQ], ALU.subtract).then_inc(S["xc_done"], 1)
                dve.wait_ge(S["xc_done"], val("xc_done", "xc", kind, s))
                dve.sem_inc(S["tr_dve"], 1)

            def var_in():
                bk = ring_in("VARp")
                dve.tensor_scalar(var[:], bk[:, 0:SEQ], 1e-5, None, ALU.add).then_inc(S["norm_in"], 1)
                dve.wait_ge(S["norm_in"], val("norm_in", "VARp", kind, s))
                dve.sem_inc(S["ring_dve"], 1)

            def norm_x():
                newton("VARp", var, y0, y1, y1, None)
                link(dve.tensor_tensor(xy[:], xc[:], y1[:], ALU.mult))
                dve.tensor_scalar(xn[:], xy[:], cur[:, 0:1], cur[:, 1:2], ALU.mult, ALU.add)\
                   .then_inc(S["xn_done"], 1)

            def gate():
                for c, (f0, n) in enumerate(FFC):
                    bk = ring_in(f"W1{'abc'[c]}p")
                    dve.wait_ge(S["ring_act"], val("ring_act", f"W1{'abc'[c]}p", kind, s))
                    dve.scalar_tensor_tensor(hh[0:n, c, :], bk[0:n, 0:SEQ], cur[0:n, 3 + c:4 + c], ge[0:n, c, :],
                                             ALU.add, ALU.mult).then_inc(S["ring_dve"], 1)

            def res_ff():
                bk = ring_in("W2p")
                x = XT[:, b_prev, 1:SEQ + 1]
                dve.scalar_tensor_tensor(x, bk[:, 0:SEQ], cur[:, 2:3], x, ALU.add, ALU.add)\
                   .then_inc(S["ring_dve"], 1)

            if nxt:
                tables()
            if ffp:
                link(dve.tensor_copy(cur[:], vecs[:, layer_p, :]))
            if kind == "pro":
                for g in range(GROUPS):
                    qk(g, 0)
                    qk(g, 1)
                norm_qk_in()
                norm_qk()
            elif kind == "tail":
                res_attention()
                center()
                var_in()
                norm_x()
                gate()
                res_ff()
            else:
                for k in range(5):
                    if ffp and k == 2:
                        norm_x()
                    if nxt:
                        if k < 3:
                            qk(k, 0)
                            if k == 0:
                                softmax(0)
                            qk(k, 1)
                        elif k == 4:
                            qk(3, 0)
                            qk(3, 1)
                            norm_qk_in()
                    if k == 0 and not nxt:
                        softmax(0)
                    if ffp and k < 4:
                        if k == 0:
                            res_attention()
                        elif k == 1:
                            center()
                        elif k == 3:
                            res_ff()
                    if ffp and k == 2:
                        gate()
                    if 0 < k < 4:
                        softmax(k)
                    if ffp and k == 1:
                        var_in()
                    if k > 0:
                        norm_o(k - 1, 0)
                        norm_o(k - 1, 1)
                if nxt:
                    norm_qk()
            assert links[0] == DVE_LINKS[kind], (kind, links[0])

        def pool_step(pool, kind, s):
            nxt = kind in ("pro", "first", "mid")

            def rotate_sum(g, tl):
                i = 2 * g + tl
                pool.wait_ge(S["ring_dve"], val("ring_dve", QK[i], kind, s))
                if kind != "pro":
                    pool.wait_ge(S["tr_full"], val("tr_full", f"{g}{tl}", kind, s))
                hd = DH // 2
                c = qc[:, tl, :].rearrange("p (h d) -> p h d", d=DH)
                n = qn[:, tl, :].rearrange("p (h d) -> p h d", d=DH)
                o = AB[:, i, :].rearrange("p (h d) -> p h d", d=DH)
                pool.tensor_tensor(o[:, :, 0:hd], c[:, :, 0:hd], n[:, :, hd:], ALU.add)
                pool.tensor_tensor(o[:, :, hd:], c[:, :, hd:], n[:, :, 0:hd], ALU.add).then_inc(S["ab_done"], 1)

            def normalise():
                pool.wait_ge(S["rinv_done"], val("rinv_done", "NRM", kind, s))
                pool.wait_ge(S["ab_done"], val("ab_done", "QK31", kind, s))
                for i in range(8):
                    o = AB[:, i, :].rearrange("p (h d) -> p h d", d=DH)
                    r = rinv[:, 8 * i:8 * i + 8].rearrange("p (h o) -> p h o", o=1).broadcast_to([P, 8, DH])
                    pool.tensor_tensor(o, o, r, ALU.mult).then_inc(S["r_done"], 1)

            if kind in ("first", "mid"):
                for k in range(3):
                    rotate_sum(k, 0)
                    rotate_sum(k, 1)
                rotate_sum(3, 0)
                rotate_sum(3, 1)
            elif kind == "pro":
                for i in range(8):
                    rotate_sum(i // 2, i % 2)
            if nxt:
                normalise()

        def whole(eng, step):
            step(eng, "pro", None)
            step(eng, "first", 0)
            with eng.Fori(1, STEPS - 1) as s:
                step(eng, "mid", s)
            step(eng, "last", STEPS - 1)
            step(eng, "tail", STEPS)

        @block.gpsimd
        def _(pool):
            pool.memset(mean[:], 1.0 / DM).then_inc(pool_set, 1)
            pool.memset(ebias[:], 8.0 * float(np.log(2.0))).then_inc(pool_set, 1)
            pool.memset(kT[:, :, :, 0:WIN], 0.0).then_inc(pool_set, 1)
            pool.memset(V[:, :, :, DH:], 1.0).then_inc(pool_set, 1)
            pool.memset(Pd[:, 0], 0.0).then_inc(pool_set, 1)
            pool.memset(Pd[:, 1], 0.0).then_inc(pool_set, 1)
            pool.memset(Pp[:], 0.0).then_inc(pool_set, 1)
            whole(pool, pool_step)

        @block.tensor
        def _(pe):
            pe.wait_ge(const_in, CONST_IN)
            pe.wait_ge(pool_set, POOL_SET)
            pe.wait_ge(mask_set, 1)
            whole(pe, pe_step)

        @block.scalar
        def _(act):
            act.preload_act_table_set(LN_EXP)
            act.wait_ge(pool_set, POOL_SET)
            whole(act, act_step)

        @block.vector
        def _(dve):
            dve.wait_ge(const_in, CONST_IN)
            dve.tensor_copy(maskb[:], xy[:])
            dve.tensor_copy(identb[:], ident[:]).then_inc(mask_set, 1)
            whole(dve, dve_step)


def gate_phase(nc, t, banks, ident, xin, XT, ST):
    with ExitStack() as ctx:
        m = Memory(nc, ctx)
        CH = NB // 2
        e = m.sb("g_exp", [P, 2, 2, SEQ])
        r = m.sb("g_den", [P, 2, 2, SEQ])
        pr = m.sb("g_prod", [P, 2, 2, SEQ])
        out = m.sb("g_out", [P, 2, 4, DM])
        e_done, link_s, p_done = m.sem("g_e_done"), m.sem("g_link"), m.sem("g_p_done")
        t_full, o_done, stored = m.sem("g_t_full"), m.sem("g_o_done"), m.sem("stored")
        block = ctx.enter_context(nc.Block())

        @block.scalar
        def _(act):
            for c in range(CH):
                if c >= 2:
                    act.wait_ge(link_s, 3 * (c - 2) + 1)
                act.activation(e[:, c % 2], XT[:, 2 * c:2 * c + 2, 1:], ACT.Exp, scale=-1.0).then_inc(e_done, 1)

        @block.vector
        def _(dve):
            def link(ins, n):
                ins.then_inc(link_s, 1)
                dve.wait_ge(link_s, n)
            for c in range(CH):
                dve.wait_ge(e_done, c + 1)
                link(dve.tensor_scalar(r[:, c % 2], e[:, c % 2], 1.0, None, ALU.add), 3 * c + 1)
                link(dve.reciprocal(r[:, c % 2], r[:, c % 2]), 3 * c + 2)
                link(dve.tensor_tensor(r[:, c % 2], r[:, c % 2], XT[:, 2 * c:2 * c + 2, 1:], ALU.mult), 3 * c + 3)
                if c >= 2:
                    dve.wait_ge(t_full, c - 1)
                dve.tensor_tensor(pr[:, c % 2], r[:, c % 2], ST[:, 2 * c:2 * c + 2, :], ALU.mult).then_inc(p_done, 1)
                dve.wait_ge(t_full, c + 1)
                if c >= 2:
                    dve.wait_ge(stored, 16 * (c - 1))
                dve.tensor_tensor(out[:, c % 2], banks[c % 2][:].rearrange("p (i n) -> p i n", n=DM),
                                  xin[:, 4 * c:4 * c + 4, :], ALU.add).then_inc(o_done, 1)

        @block.tensor
        def _(pe):
            for c in range(CH):
                pe.wait_ge(p_done, c + 1)
                if c >= 2:
                    pe.wait_ge(o_done, c - 1)
                for j in range(4):
                    mm = pe.transpose(banks[c % 2][:, j * P:(j + 1) * P],
                                      pr[:, c % 2, j // 2, (j % 2) * P:(j % 2 + 1) * P], ident[:])
                mm.then_inc(t_full, 1)

        @block.sync
        def _(sp):
            dst = t["out"].rearrange("b (i p) n -> p (b i) n", p=P)
            for c in range(CH):
                sp.wait_ge(o_done, c + 1)
                if c >= 1:
                    sp.wait_ge(stored, 16 * c)
                sp.dma_start(dst[:, 4 * c:4 * c + 4, :], out[:, c % 2]).then_inc(stored, 16)
            sp.wait_ge(stored, 16 * CH)


def bass_mamba_gated_local_transformer_kernel(nc, t):
    with ExitStack() as ctx:
        m = Memory(nc, ctx)
        ident = m.sb("ident", [P, P])
        xin = m.sb("xin", [P, NB * TILES, DM])
        XT = m.sb("XT", [P, NB, SEQ + 1])
        ST = m.sb("ST", [P, NB, SEQ])
        low = [ctx.enter_context(nc.psum_tensor(f"bank{i}", [P, 512], F32)) for i in range(3)]
        pair = ctx.enter_context(nc.psum_tensor("bank34", [P, 2, 512], F32))
        high = [ctx.enter_context(nc.psum_tensor(f"bank{i}", [P, 512], F32)) for i in range(5, 8)]
        banks = [b[:] for b in low] + [pair[:, 0], pair[:, 1]] + [b[:] for b in high]
        mamba_phase(nc, t, banks, ident, xin, XT, ST)
        transformer_phase(nc, t, banks, pair, ident, XT)
        gate_phase(nc, t, banks, ident, xin, XT, ST)


def constants():
    f = np.float32
    n = SEQ
    half = np.arange(0, DH, 2, dtype=f)
    inv_freq = (f(1.0) / np.power(f(10000.0), half / f(DH))).astype(f)
    tok = np.arange(n, dtype=f)
    fr = (tok[:, None] * inv_freq[None, :]).astype(f)
    fr = np.concatenate([fr, fr], -1)
    base_scale = (half + f(0.4 * DH)) / f(1.4 * DH)
    power = (tok - f(n // 2)) / f(WIN // 2)
    scale = np.power(base_scale[None, :], power[:, None]).astype(f)
    scale = np.concatenate([scale, scale], -1)
    cos, sin = np.cos(fr).astype(f), np.sin(fr).astype(f)
    sin = np.concatenate([sin[:, :DH // 2], -sin[:, DH // 2:]], -1)
    tab = np.zeros((P, 2, TILES, 2, DH), f)
    for c, sc in enumerate((scale, (f(1.0) / scale).astype(f))):
        for z, tr in enumerate((cos, sin)):
            tab[:, z, :, c, :] = (tr * sc).astype(f).reshape(TILES, P, DH).transpose(1, 0, 2)
    mask = np.zeros((P, TILES, GH // 2, 2 * WIN), f)
    i, j = np.arange(P)[:, None] % WIN, np.arange(2 * WIN)[None, :]
    bad = (j < i) | (j > i + WIN)
    mask[:] = np.where(bad, f(MASKED), f(0))[:, None, None, :]
    mask[0:WIN, 0, :, 0:WIN] = MASKED
    K = DTR + 2 * NST
    sel = np.zeros((K, 2 * NST, P), f)
    for r in range(2 * NST):
        sel[DTR + r, r, :] = 1.0
    return {"c_ident": np.eye(P, dtype=f), "c_mask": mask.reshape(P, -1), "c_rot": tab, "c_sel": sel}


_INS = {"x": "L0_attn_x", "rms_w": "L0_attn_rms_w", "in_W": "L0_attn_in_W", "in_b": "L0_attn_in_b",
        "conv_w": "L0_attn_conv_w", "conv_b": "L0_attn_conv_b", "A_log": "L0_attn_A_log",
        "dbc_W": "L0_attn_dbc_W", "dbc_b": "L0_attn_dbc_b", "dup_W": "L0_attn_dup_W", "dup_b": "L0_attn_dup_b",
        "out_W": "L0_attn_out_W", "out_b": "L0_attn_out_b", "Wqkv": "L0_ffn_Wqkv", "q_scale": "L0_ffn_q_scale",
        "k_scale": "L0_ffn_k_scale", "Wo": "L0_ffn_Wo", "ln_g": "L0_ffn_ln_g", "ln_b": "L0_ffn_ln_b",
        "W1": "L0_ffn_W1", "b1": "L0_ffn_b1", "W2": "L0_ffn_W2", "b2": "L0_ffn_b2"}


def mamba_vectors(g):
    def cols(a):
        return a.reshape(-1, P, *a.shape[1:]).swapaxes(0, 1).reshape(P, -1)
    return np.concatenate([cols(g[n]) for n in ("in_b", "conv_b", "dup_b", "out_b", "rms_w", "conv_w", "A_log")], 1)


def layer_vectors(g):
    v = np.zeros((P, DEPTH, NVEC), np.float32)
    for k, name in enumerate(("ln_g", "ln_b", "b2")):
        v[:, :, k] = g[name].T
    for c, (f0, n) in enumerate(FFC):
        for h in range(2):
            v[:n, :, 3 + 3 * h + c] = g["b1"][:, h * FFI + f0:h * FFI + f0 + n].T
    return v


PACKED = ("in_b", "conv_b", "dup_b", "out_b", "rms_w", "conv_w", "A_log", "ln_g", "ln_b", "b2", "b1")


def kernel(**inputs):
    import concourse.bacc as _bacc
    from concourse.bass_utils import run_bass_kernel_spmd as _run

    nc = _bacc.Bacc("TRN2", target_bir_lowering=False, num_devices=1)
    arrays, t = {}, {}
    given = {short: np.ascontiguousarray(inputs[name]) for short, name in _INS.items()}
    laid = {k: a for k, a in given.items() if k not in PACKED}
    laid["dbc_b"] = given["dbc_b"].reshape(-1, 1)
    laid["mamba_vecs"], laid["layer_vecs"] = mamba_vectors(given), layer_vectors(given)
    for short, a in {**laid, **constants()}.items():
        a = np.ascontiguousarray(a)
        arrays[f"in_{short}"] = a
        t[short] = nc.dram_tensor(f"in_{short}", a.shape, mybir.dt.from_np(a.dtype), kind="ExternalInput").ap()
    t["out"] = nc.dram_tensor("out_0", given["x"].shape, F32, kind="ExternalOutput").ap()
    bass_mamba_gated_local_transformer_kernel(nc, t)
    r = _run(nc, [arrays], core_ids=[0])
    return r.results[0]["out_0"]
```
